# Optimizing a Trainium2 kernel written in Bass

```python
import numpy as np
import jax
import jax.numpy as jnp

def _softmax(x, axis=-1):
    return jax.nn.softmax(x, axis=axis)

def _gelu(x):
    return jax.nn.gelu(x, approximate=True)

def _silu(x):
    return jax.nn.silu(x)

def _sigmoid(x):
    return jax.nn.sigmoid(x)

def _layernorm(x, axis=-1, eps=1e-05):
    m = jnp.mean(x, axis=axis, keepdims=True)
    v = jnp.var(x, axis=axis, keepdims=True)
    return (x - m) / jnp.sqrt(v + eps)

def _scatter_add(tgt, idx, src, axis=0):
    return tgt.at[idx].add(src)

def _segment_sum(src, seg, n):
    return jax.ops.segment_sum(src, seg, n)
kernel_name = 'mk_sandwich_d1_jaxref_r4_1d79c3'

def setup_inputs(seed: int=0):
    np.random.seed(seed)
    _w = jnp.asarray

    def _L0_attn_setup():
        import jax, jax.numpy as jnp
        import numpy as np
        B, S, D = (4, 512, 256)
        DK, DV = (256, 256)
        key = jax.random.key(seed)
        ks = jax.random.split(key, 5)
        x = jax.random.normal(ks[0], (B, S, D), dtype=jnp.float32)
        scale = 1.0 / np.sqrt(D)
        Wq = jax.random.normal(ks[1], (D, DK), dtype=jnp.float32) * scale
        Wk = jax.random.normal(ks[2], (D, DK), dtype=jnp.float32) * scale
        Wv = jax.random.normal(ks[3], (D, DV), dtype=jnp.float32) * scale
        Wo = jax.random.normal(ks[4], (DV, DV), dtype=jnp.float32) * (1.0 / np.sqrt(DV))
        return {'x': x, 'Wq': Wq, 'Wk': Wk, 'Wv': Wv, 'Wo': Wo}
    _L0_attn_in = _L0_attn_setup()

    def _L0_ffn_setup():
        import jax, jax.numpy as jnp
        import numpy as np
        NUM_OPS, B, T, D = (8, 8, 128, 256)
        key = jax.random.key(seed)
        k1, k2, k3, k4 = jax.random.split(key, 4)
        x = jax.random.normal(k1, (B, T, D), dtype=jnp.float32)
        W = jax.random.normal(k2, (NUM_OPS, D, D), dtype=jnp.float32) * 0.02
        b = jnp.zeros((NUM_OPS, D), dtype=jnp.float32)
        logits = 0.001 * jax.random.normal(k3, (NUM_OPS,), dtype=jnp.float32)
        u = jax.random.uniform(k4, (NUM_OPS,), dtype=jnp.float32, minval=1e-06, maxval=1.0 - 1e-06)
        return {'x': x, 'W': W, 'b': b, 'logits': logits, 'u': u}
    _L0_ffn_in = _L0_ffn_setup()
    _d = {'L0_attn_x': _L0_attn_in['x'], 'L0_attn_Wq': _L0_attn_in['Wq'], 'L0_attn_Wk': _L0_attn_in['Wk'], 'L0_attn_Wv': _L0_attn_in['Wv'], 'L0_attn_Wo': _L0_attn_in['Wo'], 'L0_ffn_W': _L0_ffn_in['W'], 'L0_ffn_b': _L0_ffn_in['b'], 'L0_ffn_logits': _L0_ffn_in['logits'], 'L0_ffn_u': _L0_ffn_in['u']}
    _x0 = _d['L0_attn_x']
    _d['L0_attn_x'] = jax.random.normal(jax.random.fold_in(jax.random.key(seed), 1), (8, 1024, 256), dtype=_x0.dtype)
    del _x0
    return _d

def reference(L0_attn_x, L0_attn_Wq, L0_attn_Wk, L0_attn_Wv, L0_attn_Wo, L0_ffn_W, L0_ffn_b, L0_ffn_logits, L0_ffn_u):

    def _L0_attn_ref(x, Wq, Wk, Wv, Wo):
        import jax, jax.numpy as jnp
        import numpy as np
        B, S, D = (4, 512, 256)
        DK, DV = (256, 256)
        dim_k = Wq.shape[1]
        q = x @ Wq
        k = x @ Wk
        v = x @ Wv
        scores = jnp.einsum('bsd,btd->bst', q, k)
        m_inf = -jnp.finfo(scores.dtype).max
        causal_mask = jnp.triu(jnp.ones((q.shape[1], q.shape[1]), dtype=bool), k=1)
        scores = jnp.where(causal_mask[None, :, :], m_inf, scores)
        attn = jax.nn.softmax(scores * dim_k ** (-0.5), axis=-1)
        out = jnp.einsum('bst,btv->bsv', attn, v) @ Wo
        return out

    def _L0_ffn_ref(x, W, b, logits, u):
        import jax, jax.numpy as jnp
        import numpy as np
        NUM_OPS, B, T, D = (8, 8, 128, 256)
        gumbel = -jnp.log(-jnp.log(u))
        idx = jnp.argmax(jax.nn.log_softmax(logits) + gumbel)
        out = jnp.einsum('btd,de->bte', x, W[idx]) + b[idx]
        return out
    x = L0_attn_x
    x = x + _layernorm(_L0_attn_ref(_layernorm(x, axis=-1), L0_attn_Wq, L0_attn_Wk, L0_attn_Wv, L0_attn_Wo), axis=-1)
    x = x + _layernorm(_L0_ffn_ref(_layernorm(x, axis=-1), L0_ffn_W, L0_ffn_b, L0_ffn_logits, L0_ffn_u), axis=-1)
    return x

_drawn_inputs = setup_inputs


def setup_inputs(seed=0):
    import zlib

    import numpy as np

    out = dict(_drawn_inputs(seed))
    spreads = {'L0_ffn_b': (0.0, 0.1)}
    factors = {}
    for name, (base, spread) in spreads.items():
        noise = np.random.default_rng([zlib.crc32(name.encode()), seed]).standard_normal(out[name].shape)
        drawn = base * np.exp(spread * noise) if base else spread * noise
        out[name] = jnp.asarray(drawn.astype(out[name].dtype))
    for name, factor in factors.items():
        out[name] = (out[name] * factor).astype(out[name].dtype)
    return out
```

```python
import concourse.bass as bass
from concourse import mybir
from contextlib import ExitStack


def sandwich_block_kernel(
    nc: bass.Bass,
    x: bass.AP,
    Wq: bass.AP,
    Wk: bass.AP,
    Wv: bass.AP,
    Wo: bass.AP,
    ffn_W: bass.AP,
    ffn_b: bass.AP,
    ffn_logits: bass.AP,
    ffn_u: bass.AP,
    out: bass.AP,
):
    f32 = mybir.dt.float32
    f32r = mybir.dt.float32r
    bf16 = mybir.dt.bfloat16
    u32 = mybir.dt.uint32
    ALU = mybir.AluOpType
    ACT = mybir.ActivationFunctionType
    AX = mybir.AxisListType

    B, S, D = x.shape
    NOPS = ffn_W.shape[0]
    PART = 128
    KC = D // PART
    NT = S // PART
    NP = NT // 2
    BANK = 512
    NB = 4
    VW = D + 2
    EPS = 1e-5
    MASKED = -1e30
    WVO_LINKS, SETUP_LINKS = 7, 15
    PAR = NT * D

    PE_ORDER = """V0 S0 V1 S1 V2 T0 S2 T1 S3 O0 T2 S4 O1 T3 S5 O2 T4 O3 S6 T5 O4 V3 Y0 S7 T6 X0 O5 F0 T7 O6 Y1
        X1 O7 Y2 F1 G0 X2 X3 F2 G1 Y3 G2 G3 F3"""
    ACT_ORDER = """V0 E0 V1 T0 E1 V2 T1 E2 T2 E3 O0 T3 O1 E4 T4 O2 E5 O3 K0 T5 H0 O4 E6 V3 Y0 H1 T6 E7 X0 O5 K1
        T7 H2 O6 F0 Y1 K2 X1 O7 Y2 H3 F1 G0 X2 X3 K3 G1 Y3 F2 G2 G3 F3"""
    DVE_ORDER = """V0 M0 M1 L0 T0 V1 M2 V2 T1 M3 T2 L1 C0 M4 C1 R0 T3 R1 N0 M5 C2 L2 R2 T4 C3 R3 M6 T5 C4 N1 V3
        Y0 R4 M7 T6 C5 X0 R5 F0 N2 T7 C6 L3 Y1 U0 R6 X1 C7 Y2 R7 F1 N3 U1 G0 X2 X3 Z0 F2 G1 Y3 Z1 U2
        G2 F3 G3 U3 Z2 Z3"""
    POOL_ORDER = """C0 C1 N0 C2 C3 L0 C4 L1 N1 L2 C5 N2 C6 L3 C7 N3 U0 U1 U2 U3"""

    def order(text, last):
        steps = [(w[0], int(w[1:])) for w in text.split()]
        return [s for s in steps if not (last and s[0] in "LHXG")]

    def t_groups(i):
        n = i + 1
        return [(0, n)] if n <= 4 else [(0, (n + 1) // 2), ((n + 1) // 2, n)]

    def pieces(i):
        w = (i + 1) * PART
        return (1, w) if w <= BANK else (2, w // 2)

    def jobs_of(steps):
        for kind, n in steps:
            if kind == "T":
                for g in range(len(t_groups(n))):
                    yield (kind, n, g)
            elif kind in "VOYFXG":
                yield (kind, n, 0)

    SPLIT = "TVYXG"
    BEFORE = [(w[0], int(w[1]), 0) for w in "X0 X1 A0 X2 X3 A1 G0 G1 G2 G3".split()]

    def is_split(job):
        return job[0] in SPLIT or job[:2] == ("A", 0)

    def places(jobs, act_jobs, job0, split0):
        splits = {j: split0 + 1 + at for at, j in enumerate(filter(is_split, act_jobs))}
        return {j: (job0 + at, splits.get(j, 0)) for at, j in enumerate(jobs)}

    before = places(BEFORE, BEFORE, 0, 0)
    JOB0, SPLIT0 = len(BEFORE), sum(map(is_split, BEFORE))
    full, final = (places(jobs_of(order(PE_ORDER, last)), jobs_of(order(ACT_ORDER, last)), JOB0, SPLIT0)
                   for last in (False, True))
    PER, SPER = len(full), sum(map(is_split, full))
    assert PER % NB == 0

    class Job:

        def __init__(self, b, last, kind, n, g=0, before=0):
            place, splits = (final if last else full)[(kind, n, g)]
            self.bank = place % NB
            self.offset = place // NB - before * (PER // NB)
            self.used = self.offset + b * (PER // NB)
            self.splits = splits + b * SPER

    class Before:
        def __init__(self, kind, n):
            place, self.splits = before[(kind, n, 0)]
            self.bank, self.offset = place % NB, place // NB
            self.used = self.offset

    def g_job(b, n):
        return Before("G", n) if isinstance(b, int) and b == 0 else Job(b, False, "G", n, before=1)

    x_rows = x.rearrange("b (t p) d -> b p t d", p=PART)
    out_rows = out.rearrange("b (t p) d -> b p t d", p=PART)

    ctx = ExitStack()
    with ctx:
        def sb(name, shape, dt=f32):
            return ctx.enter_context(nc.sbuf_tensor(name, shape, dt))

        def pb(name, shape, dt=f32):
            return ctx.enter_context(nc.psum_tensor(name, shape, dt))

        def sem(name):
            return ctx.enter_context(nc.semaphore(name))

        x_sb = sb("x_sb", [PART, 2 * PAR])
        xn = sb("xn", [PART, NT, D])
        xT_hi = sb("xT_hi", [PART, KC, S], f32r)
        xT_lo = sb("xT_lo", [PART, KC, S], f32r)
        g_hi = sb("g_hi", [PART, KC, S], f32r)
        g_lo = sb("g_lo", [PART, KC, S], f32r)
        v_hi = sb("v_hi", [PART, NT, VW], f32r)
        v_lo = sb("v_lo", [PART, NT, VW], f32r)
        probs = sb("probs", [PART, 2, S])
        pT_hi = sb("pT_hi", [PART, 2, S], f32r)
        pT_lo = sb("pT_lo", [PART, 2, S], f32r)
        y = sb("y", [PART, NT, D])
        yn = sb("yn", [PART, NP, 2, D])
        yT_hi = sb("yT_hi", [PART, NP, KC, 2 * PART], f32r)
        yT_lo = sb("yT_lo", [PART, NP, KC, 2 * PART], f32r)
        f_sb = sb("f_sb", [PART, NP, 2, D])
        out_sb = sb("out_sb", [PART, NP, 2, D])
        squares_junk = sb("squares_junk", [PART, 2, NT, D], bf16)
        neg_max = sb("neg_max", [PART, NT])
        x_stats = sb("x_stats", [PART, NT, 6])
        x_mv = sb("x_mv", [PART, NT, 2])
        x_ve = sb("x_ve", [PART, NT])
        x_nm = sb("x_nm", [PART, NT])
        x_rstd = sb("x_rstd", [PART, NT])
        x_shift = sb("x_shift", [PART, NT])
        o_ss = sb("o_ss", [PART, NT])
        o_ez = sb("o_ez", [PART, NT])
        o_ve = sb("o_ve", [PART, NT])
        o_rstd = sb("o_rstd", [PART, NT])
        y_stats = sb("y_stats", [PART, NT, 6])
        y_mv = sb("y_mv", [PART, NT, 2])
        y_ve = sb("y_ve", [PART, NT])
        y_nm = sb("y_nm", [PART, NT])
        y_shift = sb("y_shift", [PART, NT])
        y_rstd = sb("y_rstd", [PART, NT])
        f_ss = sb("f_ss", [PART, NT])
        f_ve = sb("f_ve", [PART, NT])
        f_rstd = sb("f_rstd", [PART, NT])
        minus_half = sb("minus_half", [PART, NT])
        wq = sb("wq", [PART, KC, D])
        wk = sb("wk", [PART, KC, D])
        wv = sb("wv", [PART, KC, D])
        wo = sb("wo", [PART, KC, D])
        wT = sb("wT", [PART, 3, KC, D])
        a_hi = sb("a_hi", [PART, KC, D], f32r)
        a_lo = sb("a_lo", [PART, KC, D], f32r)
        wvo = sb("wvo", [PART, KC, D])
        wvo_hi = sb("wvo_hi", [PART, KC, D], f32r)
        wvo_lo = sb("wvo_lo", [PART, KC, D], f32r)
        wf = sb("wf", [PART, KC, D])
        wf_hi = sb("wf_hi", [PART, KC, D], f32r)
        wf_lo = sb("wf_lo", [PART, KC, D], f32r)
        bias = sb("bias", [PART, D])
        row_sum = sb("row_sum", [PART, 5])
        row_mean = sb("row_mean", [PART, 5])
        ident = sb("ident", [PART, PART])
        ident_b = sb("ident_b", [PART, PART], bf16)
        mask_b = sb("mask_b", [PART, PART], bf16)
        logits = sb("logits", [1, NOPS])
        noise_u = sb("noise_u", [1, NOPS])
        log_u = sb("log_u", [1, NOPS])
        neg_gumbel = sb("neg_gumbel", [1, NOPS])
        exp_logits = sb("exp_logits", [1, NOPS])
        lse = sb("lse", [1, 3])
        noisy = sb("noisy", [1, NOPS])
        top8 = sb("top8", [1, 8])
        chosen = sb("chosen", [1, 8], u32)

        score = pb("score", [PART, 2, 2, BANK])
        bank = [pb(f"bank{i}", [PART, BANK]) for i in range(NB)]

        bank_full = [sem(f"bank_full{i}") for i in range(NB)]
        bank_drained = [sem(f"bank_drained{i}") for i in range(NB)]
        hi_ready = sem("hi_ready")
        scores_ready = sem("scores_ready")
        max_ready = sem("max_ready")
        probs_ready = sem("probs_ready")
        o_squares = sem("o_squares")
        o_ve_ready = sem("o_ve_ready")
        o_rstd_ready = sem("o_rstd_ready")
        y_mv_ready = sem("y_mv_ready")
        y_ve_ready = sem("y_ve_ready")
        y_shift_ready = sem("y_shift_ready")
        yn_ready = sem("yn_ready")
        f_squares = sem("f_squares")
        f_ve_ready = sem("f_ve_ready")
        f_rstd_ready = sem("f_rstd_ready")
        out_ready = sem("out_ready")
        out_sent = [sem(f"out_sent{i}") for i in range(NP)]
        x_loaded = [sem(f"x_loaded{i}") for i in range(NP)]
        x_mv_ready = sem("x_mv_ready")
        x_ve_ready = sem("x_ve_ready")
        x_shift_ready = sem("x_shift_ready")
        xn_ready = sem("xn_ready")
        wq_loaded = sem("wq_loaded")
        wk_loaded = sem("wk_loaded")
        wv_loaded = sem("wv_loaded")
        wo_loaded = sem("wo_loaded")
        choice_loaded = sem("choice_loaded")
        wf_loaded = sem("wf_loaded")
        memsets = sem("memsets")
        consts_ready = sem("consts_ready")
        w_transposed = sem("w_transposed")
        wT_ready = sem("wT_ready")
        setup_steps = sem("setup_steps")
        choice_act = sem("choice_act")
        choice_dve = sem("choice_dve")
        chosen_ready = sem("chosen_ready")

        block = ctx.enter_context(nc.Block())

        def cols(bk, n=BANK):
            return bank[bk][:, 0:n]

        def x_tile(b, t, n=1):
            return x_sb[:, bass.ds((b % 2) * PAR + t * D, n * D)]

        @block.sync
        def _(sp):
            def load_x(b, p, parity_at):
                sp.dma_start(x_sb[:, bass.ds(parity_at + 2 * p * D, 2 * D)],
                             x_rows[b, :, 2 * p:2 * p + 2, :]).then_inc(x_loaded[p], 16)

            def store(b, p):
                sp.wait_ge(out_ready, b * NP + p + 1)
                sp.dma_start(out_rows[b, :, 2 * p:2 * p + 2, :], out_sb[:, p]).then_inc(out_sent[p], 16)

            def weight(w_sb, w_dram, loaded):
                sp.dma_start(w_sb[:, :, :], w_dram.rearrange("(k p) n -> p k n", p=PART)).then_inc(loaded, 16)

            load_x(0, 0, 0)
            load_x(0, 1, 0)
            weight(wq, Wq, wq_loaded)
            weight(wk, Wk, wk_loaded)
            load_x(0, 2, 0)
            load_x(0, 3, 0)
            weight(wv, Wv, wv_loaded)
            weight(wo, Wo, wo_loaded)
            sp.wait_ge(chosen_ready, 1)
            op = sp.value_load(chosen[0:1, 0:1], min_val=0, max_val=NOPS - 1)
            sp.dma_start(wf[:, :, :], ffn_W[bass.ds(op, 1), :, :].rearrange("o (k p) n -> p (o k) n", p=PART)
                         ).then_inc(wf_loaded, 16)
            sp.dma_start(bias[:, :], ffn_b[bass.ds(op, 1), :].broadcast_to([PART, D])).then_inc(wf_loaded, 16)
            for p in range(NP):
                sp.wait_ge(x_loaded[p], 16)
                load_x(1, p, PAR)

            def load_after(b, p):
                added = Job(b, False, "O", 2 * p + 1)
                sp.wait_ge(bank_drained[added.bank], added.used + 1)
                load_x(b + 2, p, (b % 2) * PAR)

            def sequence(b):
                for p in range(NP):
                    load_after(b, p)
                for p in range(NP):
                    store(b, p)

            sequence(0)
            with sp.Fori(1, B - 2) as b:
                sequence(b)
            for b in (B - 2, B - 1):
                for p in range(NP):
                    store(b, p)
            for p in range(NP):
                sp.wait_ge(out_sent[p], 16 * B)

        @block.gpsimd
        def _(pool):
            nc.gpsimd.memset(ident[:, :], 0.0)
            nc.gpsimd.memset(ident_b[:, :], 0.0)
            nc.gpsimd.memset(mask_b[:, :], 0.0).then_inc(memsets, 1)
            pool.wait_ge(memsets, 1)
            for eye in (ident, ident_b):
                nc.gpsimd.affine_select(out=eye[:, :], in_=eye[:, :], compare_op=ALU.not_equal, fill=1.0, base=0,
                                        pattern=[[-1, PART]], channel_multiplier=1)
            nc.gpsimd.affine_select(out=mask_b[:, :], in_=mask_b[:, :], compare_op=ALU.is_ge, fill=MASKED, base=0,
                                    pattern=[[-1, PART]], channel_multiplier=1).then_inc(consts_ready, 1)
            nc.gpsimd.memset(minus_half[:, :], -0.5)
            for half, one in ((v_hi, 1.0), (v_lo, 0.0)):
                nc.gpsimd.memset(half[:, :, D:D + 1].bitcast(f32), one)
                last = nc.gpsimd.memset(half[:, :, D + 1:D + 2].bitcast(f32), 0.0)
            last.then_inc(memsets, 1)
            pool.wait_ge(memsets, 2)

            def rstd(dst, ve, n0, n1):
                return nc.gpsimd.tensor_tensor(dst[:, n0:n1], ve[:, n0:n1], minus_half[:, n0:n1], ALU.pow)

            def scales(nm, ve, rstds, shift, p):
                rstd(rstds, ve, 2 * p, 2 * p + 2)
                pool.drain()
                return nc.gpsimd.tensor_tensor(shift[:, 2 * p:2 * p + 2], nm[:, 2 * p:2 * p + 2],
                                               rstds[:, 2 * p:2 * p + 2], ALU.mult)

            def x_scales(b, p):
                pool.wait_ge(x_ve_ready, b * NP + p + 1)
                scales(x_nm, x_ve, x_rstd, x_shift, p).then_inc(x_shift_ready, 1)

            def sequence(b, last_one=False):
                for kind, n in order(POOL_ORDER, last_one):
                    if kind == "L":
                        x_scales(b + 1, n)
                    elif kind == "C":
                        pool.wait_ge(o_ve_ready, b * NT + n + 1)
                        rstd(o_rstd, o_ve, n, n + 1).then_inc(o_rstd_ready, 1)
                    elif kind == "N":
                        pool.wait_ge(y_ve_ready, b * NP + n + 1)
                        scales(y_nm, y_ve, y_rstd, y_shift, n).then_inc(y_shift_ready, 1)
                    elif kind == "U":
                        pool.wait_ge(f_ve_ready, b * NP + n + 1)
                        rstd(f_rstd, f_ve, 2 * n, 2 * n + 2).then_inc(f_rstd_ready, 1)

            for p in range(NP):
                x_scales(0, p)
            sequence(0)
            with pool.Fori(1, B - 1) as b:
                sequence(b)
            sequence(B - 1, True)

        @block.scalar
        def _(act):
            act.dma_start(logits[:, :], ffn_logits[None, :]).then_inc(choice_loaded, 16)
            act.dma_start(noise_u[:, :], ffn_u[None, :]).then_inc(choice_loaded, 16)
            act.wait_ge(choice_loaded, 32)
            nc.scalar.activation(log_u[:, :], noise_u[:, :], ACT.Ln).then_inc(choice_act, 1)
            act.wait_ge(choice_act, 1)
            nc.scalar.activation(neg_gumbel[:, :], log_u[:, :], ACT.Ln, scale=-1.0)
            act.wait_ge(choice_dve, 1)
            nc.scalar.activation(exp_logits[:, :], logits[:, :], ACT.Exp, bias=lse[:, 0:1],
                                 accum_out=lse[:, 1:2]).then_inc(choice_act, 1)
            act.wait_ge(choice_act, 2)
            nc.scalar.activation(lse[:, 2:3], lse[:, 1:2], ACT.Ln).then_inc(choice_act, 1)

            def round_hi(job, dst, src):
                act.wait_ge(bank_full[job.bank], job.used + 1)
                nc.scalar.activation(dst, src, ACT.Identity).then_inc(hi_ready, 1)

            def x_hi(job, p):
                round_hi(job, xT_hi[:, :, 2 * p * PART:2 * (p + 1) * PART],
                         cols(job.bank).rearrange("p (k s) -> p k s", k=KC))

            def g_hi_quarter(job, n):
                c, m = n // 2, n % 2
                round_hi(job, g_hi[:, m, c * BANK:(c + 1) * BANK], cols(job.bank))

            def normalise_x(b, p):
                act.wait_ge(x_shift_ready, b * NP + p + 1)
                for t in (2 * p, 2 * p + 1):
                    last = nc.scalar.activation(xn[:, t, :], x_tile(b, t), ACT.Identity, bias=x_shift[:, t:t + 1],
                                                scale=x_rstd[:, t:t + 1])
                last.then_inc(xn_ready, 1)

            normalise_x(0, 0)
            normalise_x(0, 1)
            for kind, n, _g in BEFORE:
                if kind == "A" and n == 0:
                    normalise_x(0, 2)
                    normalise_x(0, 3)
                if kind == "X":
                    x_hi(Before("X", n), n)
                elif kind == "G":
                    g_hi_quarter(Before("G", n), n)
                elif n == 0:
                    job = Before("A", 0)
                    act.wait_ge(bank_full[job.bank], job.used + 1)
                    nc.scalar.activation(a_hi[:, :, :], cols(job.bank).rearrange("p (m n) -> p m n", m=KC),
                                         ACT.Identity, scale=float(D) ** -0.5).then_inc(hi_ready, 1)

            def sequence(b, last_one=False):
                def at(kind, n, g=0):
                    return Job(b, last_one, kind, n, g)

                for kind, n in order(ACT_ORDER, last_one):
                    if kind == "E":
                        act.wait_ge(max_ready, b * NT + n + 1)
                        h, w = pieces(n)
                        nc.scalar.activation(probs[:, n % 2, 0:h * w].rearrange("p (h w) -> p h w", h=h),
                                             score[:, n % 2, 0:h, 0:w], ACT.Exp,
                                             bias=neg_max[:, n:n + 1]).then_inc(probs_ready, 1)
                    elif kind == "T":
                        for g, (t0, t1) in enumerate(t_groups(n)):
                            job = at("T", n, g)
                            round_hi(job, pT_hi[:, n % 2, t0 * PART:t1 * PART], cols(job.bank, (t1 - t0) * PART))
                    elif kind == "V":
                        job = at("V", n)
                        round_hi(job, v_hi[:, 2 * n:2 * n + 2, 0:D],
                                 cols(job.bank).rearrange("p (t d) -> p t d", t=2))
                    elif kind == "Y":
                        job = at("Y", n)
                        round_hi(job, yT_hi[:, n, :, :], cols(job.bank).rearrange("p (k s) -> p k s", k=KC))
                    elif kind == "H":
                        normalise_x(b + 1, n)
                    elif kind == "X":
                        x_hi(at("X", n), n)
                    elif kind == "G":
                        g_hi_quarter(at("G", n), n)
                    elif kind == "O":
                        job = at("O", n)
                        act.wait_ge(bank_full[job.bank], job.used + 1)
                        nc.scalar.activation(squares_junk[:, 0, n, :], cols(job.bank, D), ACT.Square,
                                             accum_out=o_ss[:, n:n + 1])
                        nc.scalar.activation(o_ez[:, n:n + 1], bank[job.bank][:, D:D + 1], ACT.Square,
                                             scale=EPS ** 0.5).then_inc(o_squares, 1)
                    elif kind == "K":
                        act.wait_ge(y_shift_ready, b * NP + n + 1)
                        for t in (2 * n, 2 * n + 1):
                            last = nc.scalar.activation(yn[:, n, t % 2, :], y[:, t, :], ACT.Identity,
                                                        bias=y_shift[:, t:t + 1], scale=y_rstd[:, t:t + 1])
                        last.then_inc(yn_ready, 1)
                    elif kind == "F":
                        job = at("F", n)
                        act.wait_ge(bank_drained[job.bank], job.used + 1)
                        for t in range(2):
                            last = nc.scalar.activation(squares_junk[:, 1, 2 * n + t, :], f_sb[:, n, t, :], ACT.Square,
                                                        accum_out=f_ss[:, 2 * n + t:2 * n + t + 1])
                        last.then_inc(f_squares, 1)

            sequence(0)
            with act.Fori(1, B - 1) as b:
                sequence(b)
            sequence(B - 1, True)

        @block.vector
        def _(dve):
            links = [0]

            def link(ins):
                links[0] += 1
                ins.then_inc(setup_steps, 1)
                dve.wait_ge(setup_steps, links[0])

            def subtract_lo(job, dst, hi, src):
                dve.wait_ge(hi_ready, job.splits)
                nc.vector.tensor_tensor(dst, src, hi.bitcast(f32), ALU.subtract).then_inc(bank_drained[job.bank], 1)

            def x_lo(job, p):
                here = slice(2 * p * PART, 2 * (p + 1) * PART)
                subtract_lo(job, xT_lo[:, :, here], xT_hi[:, :, here], cols(job.bank).rearrange("p (k s) -> p k s", k=KC))

            def g_lo_quarter(job, n):
                m, here = n % 2, slice(n // 2 * BANK, (n // 2 + 1) * BANK)
                subtract_lo(job, g_lo[:, m, here], g_hi[:, m, here], cols(job.bank))

            def x_statistics(b, p):
                dve.wait_ge(x_loaded[p], 16 * (b + 1))
                for t in (2 * p, 2 * p + 1):
                    nc.vector.bn_stats(x_stats[:, t, :], x_tile(b, t))
                dve.drain()
                for t in (2 * p, 2 * p + 1):
                    last = nc.vector.bn_aggr(x_mv[:, t, :], x_stats[:, t, :])
                last.then_inc(x_mv_ready, 1)
                dve.wait_ge(x_mv_ready, b * NP + p + 1)
                nc.vector.tensor_scalar(x_nm[:, 2 * p:2 * p + 2], x_mv[:, 2 * p:2 * p + 2, 0], -1.0, None, ALU.mult)
                nc.vector.tensor_scalar(x_ve[:, 2 * p:2 * p + 2], x_mv[:, 2 * p:2 * p + 2, 1], EPS, None,
                                        ALU.add).then_inc(x_ve_ready, 1)

            def centre(w, n):
                link(nc.vector.reduce_sum(row_sum[:, n:n + KC], w, AX.X))
                link(nc.vector.tensor_scalar(row_mean[:, n:n + KC], row_sum[:, n:n + KC], 1.0 / D, None, ALU.mult))

            def split(w, hi, lo):
                link(nc.vector.tensor_copy(hi[:, :, :], w[:, :, :]))
                link(nc.vector.tensor_tensor(lo[:, :, :], w[:, :, :], hi[:, :, :].bitcast(f32), ALU.subtract))

            x_statistics(0, 0)
            dve.wait_ge(choice_loaded, 32)
            nc.vector.tensor_reduce(lse[:, 0:1], logits[:, :], AX.X, ALU.max, negate=True).then_inc(choice_dve, 1)
            for n, (w_from, w_loaded) in enumerate(((wq, wq_loaded), (wk, wk_loaded), (wv, wv_loaded))):
                dve.wait_ge(w_transposed, n + 1)
                nc.vector.tensor_copy(wT[:, n, :, :].rearrange("p k n -> p (k n)"),
                                      score[:, n // 2, n % 2, :]).then_inc(wT_ready, 1)
                x_statistics(0, n + 1)
            dve.wait_ge(choice_act, 3)
            link(nc.vector.tensor_scalar(noisy[:, :], logits[:, :], lse[:, 0:1], lse[:, 2:3], ALU.add, ALU.subtract))
            link(nc.vector.tensor_tensor(noisy[:, :], noisy[:, :], neg_gumbel[:, :], ALU.subtract))
            link(nc.vector.max(top8[:, :], noisy[:, :]))
            nc.vector.max_index(chosen[:, :], top8[:, :], noisy[:, :]).then_inc(chosen_ready, 1)
            for kind, n, _g in BEFORE:
                job = Before(kind, n)
                if kind == "X":
                    x_lo(job, n)
                elif kind == "G":
                    g_lo_quarter(job, n)
                elif n == 0:
                    dve.wait_ge(hi_ready, job.splits)
                    nc.vector.scalar_tensor_tensor(out=a_lo[:, :, :], in0=cols(job.bank).rearrange("p (m n) -> p m n", m=KC),
                                                   scalar=float(D) ** -0.5, in1=a_hi[:, :, :].bitcast(f32),
                                                   op0=ALU.mult, op1=ALU.subtract).then_inc(bank_drained[job.bank], 1)
                else:
                    dve.wait_ge(bank_full[job.bank], job.used + 1)
                    centre(cols(job.bank).rearrange("p (m n) -> p m n", m=KC), 0)
                    for m in range(KC):
                        last = nc.vector.tensor_scalar(wvo[:, m, :], cols(job.bank)[:, m * D:(m + 1) * D],
                                                       row_mean[:, m:m + 1], None, ALU.subtract)
                    last.then_inc(bank_drained[job.bank], 1)
                    dve.wait_ge(bank_drained[job.bank], job.used + 1)
                    split(wvo, wvo_hi, wvo_lo)
                    wvo_links = links[0]
            dve.wait_ge(wf_loaded, 32)
            centre(wf[:, :, :], 2)
            for m in range(KC):
                last = nc.vector.tensor_scalar(wf[:, m, :], wf[:, m, :], row_mean[:, 2 + m:3 + m], None, ALU.subtract)
            link(last)
            split(wf, wf_hi, wf_lo)
            link(nc.vector.reduce_sum(row_sum[:, 4:5], bias[:, :], AX.X))
            link(nc.vector.tensor_scalar(row_mean[:, 4:5], row_sum[:, 4:5], 1.0 / D, None, ALU.mult))
            link(nc.vector.tensor_scalar(bias[:, :], bias[:, :], row_mean[:, 4:5], None, ALU.subtract))
            assert links[0] == SETUP_LINKS and wvo_links == WVO_LINKS

            def sequence(b, last_one=False):
                def at(kind, n, g=0):
                    return Job(b, last_one, kind, n, g)

                for kind, n in order(DVE_ORDER, last_one):
                    if kind == "M":
                        dve.wait_ge(scores_ready, b * NT + n + 1)
                        h, w = pieces(n)
                        nc.vector.tensor_reduce(neg_max[:, n:n + 1], score[:, n % 2, 0:h, 0:w], AX.XY if h > 1 else AX.X,
                                                ALU.max, negate=True).then_inc(max_ready, 1)
                    elif kind == "T":
                        for g, (t0, t1) in enumerate(t_groups(n)):
                            job, here = at("T", n, g), slice(t0 * PART, t1 * PART)
                            subtract_lo(job, pT_lo[:, n % 2, here], pT_hi[:, n % 2, here],
                                        cols(job.bank, (t1 - t0) * PART))
                    elif kind == "V":
                        job = at("V", n)
                        subtract_lo(job, v_lo[:, 2 * n:2 * n + 2, 0:D], v_hi[:, 2 * n:2 * n + 2, 0:D],
                                    cols(job.bank).rearrange("p (t d) -> p t d", t=2))
                    elif kind == "Y":
                        job = at("Y", n)
                        subtract_lo(job, yT_lo[:, n, :, :], yT_hi[:, n, :, :],
                                    cols(job.bank).rearrange("p (k s) -> p k s", k=KC))
                    elif kind == "X":
                        x_lo(at("X", n), n)
                    elif kind == "G":
                        g_lo_quarter(at("G", n), n)
                    elif kind == "L":
                        x_statistics(b + 1, n)
                    elif kind == "C":
                        dve.wait_ge(o_squares, b * NT + n + 1)
                        nc.vector.tensor_scalar(o_ve[:, n:n + 1], o_ss[:, n:n + 1], 1.0 / D, o_ez[:, n:n + 1],
                                                ALU.mult, ALU.add).then_inc(o_ve_ready, 1)
                    elif kind == "R":
                        job = at("O", n)
                        dve.wait_ge(o_rstd_ready, b * NT + n + 1)
                        nc.vector.scalar_tensor_tensor(out=y[:, n, :], in0=cols(job.bank, D), scalar=o_rstd[:, n:n + 1],
                                                       in1=x_tile(b, n), op0=ALU.mult,
                                                       op1=ALU.add).then_inc(bank_drained[job.bank], 1)
                    elif kind == "N":
                        for t in (2 * n, 2 * n + 1):
                            job = at("O", t)
                            dve.wait_ge(bank_drained[job.bank], job.used + 1)
                            nc.vector.bn_stats(y_stats[:, t, :], y[:, t, :])
                        dve.drain()
                        for t in (2 * n, 2 * n + 1):
                            last = nc.vector.bn_aggr(y_mv[:, t, :], y_stats[:, t, :])
                        last.then_inc(y_mv_ready, 1)
                        dve.wait_ge(y_mv_ready, b * NP + n + 1)
                        nc.vector.tensor_scalar(y_nm[:, 2 * n:2 * n + 2], y_mv[:, 2 * n:2 * n + 2, 0], -1.0, None,
                                                ALU.mult)
                        nc.vector.tensor_scalar(y_ve[:, 2 * n:2 * n + 2], y_mv[:, 2 * n:2 * n + 2, 1], EPS, None,
                                                ALU.add).then_inc(y_ve_ready, 1)
                    elif kind == "F":
                        job = at("F", n)
                        dve.wait_ge(bank_full[job.bank], job.used + 1)
                        nc.vector.tensor_tensor(f_sb[:, n, :, :], cols(job.bank).rearrange("p (t d) -> p t d", t=2),
                                                bias[:, None, :].broadcast_to([PART, 2, D]),
                                                ALU.add).then_inc(bank_drained[job.bank], 1)
                    elif kind == "U":
                        dve.wait_ge(f_squares, b * NP + n + 1)
                        nc.vector.tensor_scalar(f_ve[:, 2 * n:2 * n + 2], f_ss[:, 2 * n:2 * n + 2], 1.0 / D, EPS,
                                                ALU.mult, ALU.add).then_inc(f_ve_ready, 1)
                    elif kind == "Z":
                        if not (isinstance(b, int) and b == 0):
                            dve.wait_ge(out_sent[n], b * 16)
                        dve.wait_ge(f_rstd_ready, b * NP + n + 1)
                        for t in (2 * n, 2 * n + 1):
                            last = nc.vector.scalar_tensor_tensor(out=out_sb[:, n, t % 2, :], in0=f_sb[:, n, t % 2, :],
                                                                  scalar=f_rstd[:, t:t + 1], in1=y[:, t, :],
                                                                  op0=ALU.mult, op1=ALU.add)
                        last.then_inc(out_ready, 1)

            sequence(0)
            with dve.Fori(1, B - 1) as b:
                sequence(b)
            sequence(B - 1, True)

        @block.tensor
        def _(pe):
            def take_bank(job, *inputs):
                needed = {job.bank: (job.offset, job.used)} if job.offset else {}
                for done in inputs:
                    if done.offset + 1 > needed.get(done.bank, (0,))[0]:
                        needed[done.bank] = (done.offset + 1, done.used + 1)
                for bk, (_offset, used) in needed.items():
                    pe.wait_ge(bank_drained[bk], used)

            def product(dst, halves_l, halves_r):
                passes = [(l, r) for (l_hi, l_lo), (r_hi, r_lo) in zip(halves_l, halves_r)
                          for l, r in ((l_lo, r_hi), (l_hi, r_lo), (l_hi, r_hi))]
                for i, (l, r) in enumerate(passes):
                    last = nc.tensor.matmul(dst, l, r, start=(i == 0), stop=(i == len(passes) - 1))
                return last

            def both(hi, lo, *index):
                return hi[index], lo[index]

            ALL = slice(None)

            def x_transposes(b, job, p):
                pe.wait_ge(xn_ready, b * NP + p + 1)
                take_bank(job)
                for k in range(KC):
                    for t in range(2):
                        last = nc.tensor.transpose(cols(job.bank)[:, (2 * k + t) * PART:(2 * k + t + 1) * PART],
                                                   xn[:, 2 * p + t, k * PART:(k + 1) * PART], ident[:, :])
                last.then_inc(bank_full[job.bank], 1)

            def g_quarter(job, inputs, n):
                c, m = n // 2, n % 2
                take_bank(job, *inputs)
                product(cols(job.bank),
                        [both(a_hi, a_lo, ALL, k, slice(m * PART, (m + 1) * PART)) for k in range(KC)],
                        [both(xT_hi, xT_lo, ALL, k, slice(c * BANK, (c + 1) * BANK)) for k in range(KC)]
                        ).then_inc(bank_full[job.bank], 1)

            pe.wait_ge(consts_ready, 1)
            for n, (w, loaded) in enumerate(((wq, wq_loaded), (wk, wk_loaded), (wv, wv_loaded))):
                pe.wait_ge(loaded, 16)
                for k in range(KC):
                    for m in range(KC):
                        last = nc.tensor.transpose(score[:, n // 2, n % 2, (2 * k + m) * PART:(2 * k + m + 1) * PART],
                                                   w[:, m, k * PART:(k + 1) * PART], ident[:, :])
                last.then_inc(w_transposed, 1)
            for kind, n, _g in BEFORE:
                job = Before(kind, n)
                if kind == "X":
                    x_transposes(0, job, n)
                elif kind == "G":
                    g_quarter(job, [Before("A", 0), Before("X", 2 * (n // 2)), Before("X", 2 * (n // 2) + 1)], n)
                else:
                    pe.wait_ge(wT_ready, 2 + n)
                    if n:
                        pe.wait_ge(wo_loaded, 16)
                    take_bank(job)
                    for m in range(KC):
                        for k in range(KC):
                            last = nc.tensor.matmul(cols(job.bank)[:, m * D:(m + 1) * D],
                                                    wT[:, 2 * n, k, m * PART:(m + 1) * PART],
                                                    wo[:, k, :] if n else wT[:, 1, k, :],
                                                    start=(k == 0), stop=(k == KC - 1))
                    last.then_inc(bank_full[job.bank], 1)
            pe.wait_ge(setup_steps, WVO_LINKS)
            pe.wait_ge(memsets, 2)

            def sequence(b, last_one=False, first=False):
                def at(kind, n, g=0):
                    return Job(b, last_one, kind, n, g)

                for kind, n in order(PE_ORDER, last_one):
                    if kind == "S":
                        if n == 0 or n == NT // 2:
                            g = g_job(b, 2 * (n // (NT // 2)) + 1)
                            pe.wait_ge(bank_drained[g.bank], g.used + 1)
                        h, w = pieces(n)
                        for piece in range(h):
                            wide = max(w, 2 * PART)
                            last = product(score[:, n % 2, piece, 0:wide],
                                           [both(g_hi, g_lo, ALL, k, slice(n * PART, (n + 1) * PART)) for k in range(KC)],
                                           [both(xT_hi, xT_lo, ALL, k, slice(piece * w, piece * w + wide))
                                            for k in range(KC)])
                        nc.tensor.matmul(score[:, n % 2, h - 1, w - PART:w], ident_b[:, :], mask_b[:, :],
                                         start=False, stop=True, skip_group_check=True).then_inc(scores_ready, 1)
                    elif kind == "T":
                        pe.wait_ge(probs_ready, b * NT + n + 1)
                        for g, (t0, t1) in enumerate(t_groups(n)):
                            job = at("T", n, g)
                            take_bank(job)
                            for t in range(t0, t1):
                                last = nc.tensor.transpose(cols(job.bank)[:, (t - t0) * PART:(t - t0 + 1) * PART],
                                                           probs[:, n % 2, t * PART:(t + 1) * PART], ident[:, :])
                            last.then_inc(bank_full[job.bank], 1)
                    elif kind == "V":
                        job = at("V", n)
                        take_bank(job)
                        for t in (2 * n, 2 * n + 1):
                            last = product(cols(job.bank)[:, t % 2 * D:(t % 2 + 1) * D],
                                           [both(xT_hi, xT_lo, ALL, k, slice(t * PART, (t + 1) * PART)) for k in range(KC)],
                                           [both(wvo_hi, wvo_lo, ALL, k, ALL) for k in range(KC)])
                        last.then_inc(bank_full[job.bank], 1)
                    elif kind == "O":
                        job = at("O", n)
                        take_bank(job, at("T", n, len(t_groups(n)) - 1), at("V", n // 2))
                        product(cols(job.bank, VW),
                                [both(pT_hi, pT_lo, ALL, n % 2, slice(t * PART, (t + 1) * PART)) for t in range(n + 1)],
                                [both(v_hi, v_lo, ALL, t, ALL) for t in range(n + 1)]
                                ).then_inc(bank_full[job.bank], 1)
                    elif kind == "Y":
                        pe.wait_ge(yn_ready, b * NP + n + 1)
                        job = at("Y", n)
                        take_bank(job)
                        for k in range(KC):
                            for t in range(2):
                                last = nc.tensor.transpose(cols(job.bank)[:, (2 * k + t) * PART:(2 * k + t + 1) * PART],
                                                           yn[:, n, t, k * PART:(k + 1) * PART], ident[:, :])
                        last.then_inc(bank_full[job.bank], 1)
                    elif kind == "F":
                        if first and n == 0:
                            pe.wait_ge(setup_steps, SETUP_LINKS)
                        job = at("F", n)
                        take_bank(job, at("Y", n))
                        for t in range(2):
                            last = product(cols(job.bank)[:, t * D:(t + 1) * D],
                                           [both(yT_hi, yT_lo, ALL, n, k, slice(t * PART, (t + 1) * PART))
                                            for k in range(KC)],
                                           [both(wf_hi, wf_lo, ALL, k, ALL) for k in range(KC)])
                        last.then_inc(bank_full[job.bank], 1)
                    elif kind == "X":
                        x_transposes(b + 1, at("X", n), n)
                    elif kind == "G":
                        g_quarter(at("G", n), [at("X", 2 * (n // 2) + 1)], n)

            sequence(0, first=True)
            with pe.Fori(1, B - 1) as b:
                sequence(b)
            sequence(B - 1, last_one=True)


_INS = ["L0_attn_x", "L0_attn_Wq", "L0_attn_Wk", "L0_attn_Wv", "L0_attn_Wo",
        "L0_ffn_W", "L0_ffn_b", "L0_ffn_logits", "L0_ffn_u"]
_OUTS = [((8, 1024, 256), "float32")]


def kernel(**inputs):
    import numpy as _np
    import concourse.bacc as _bacc
    from concourse import mybir as _mybir
    from concourse.bass_utils import run_bass_kernel_spmd as _run

    nc = _bacc.Bacc("TRN2", target_bir_lowering=False, num_devices=1)
    arrays, args = {}, []
    for name in _INS:
        a = _np.ascontiguousarray(inputs[name])
        arrays[f"in_{name}_dram"] = a
        args.append(nc.dram_tensor(f"in_{name}_dram", a.shape, _mybir.dt.from_np(a.dtype), kind="ExternalInput").ap())
    for i, (shape, dtype) in enumerate(_OUTS):
        dt = _mybir.dt.from_np(_np.dtype(dtype))
        args.append(nc.dram_tensor(f"out_{i}_dram", shape, dt, kind="ExternalOutput").ap())
    sandwich_block_kernel(nc, *args)
    r = _run(nc, [arrays], core_ids=[0])
    got = tuple(r.results[0][f"out_{i}_dram"] for i in range(len(_OUTS)))
    return got[0]
```

```python
import concourse.bass as bass
from concourse import mybir
from contextlib import ExitStack


def sandwich_block_kernel(
    nc: bass.Bass,
    x: bass.AP,
    Wq: bass.AP,
    Wk: bass.AP,
    Wv: bass.AP,
    Wo: bass.AP,
    ffn_W: bass.AP,
    ffn_b: bass.AP,
    ffn_logits: bass.AP,
    ffn_u: bass.AP,
    out: bass.AP,
):
    f32 = mybir.dt.float32
    f32r = mybir.dt.float32r
    bf16 = mybir.dt.bfloat16
    u32 = mybir.dt.uint32
    ALU = mybir.AluOpType
    ACT = mybir.ActivationFunctionType
    AX = mybir.AxisListType

    B, S, D = x.shape
    NOPS = ffn_W.shape[0]
    PART = 128
    KC = D // PART
    NT = S // PART
    NP = NT // 2
    BANK = 512
    NB = 4
    EPS = 1e-5
    MASKED = 1e30
    SCALE = float(D) ** -0.5
    PAR = NT * D

    PE_ORDER = """S0 V0 S1 V1 T0 S2 T1 S3 O0 V2 T2 O1 S4 T3 V3 O2 S5 O3 T4 S6 T5 S7 X0 Y0 O4 T6 O5 T7 O6 X1 Y1
        O7 F0 G0 Y2 X2 F1 X3 F2 Y3 G1 G2 F3 G3"""
    ACT_ORDER = """V0 E0 E1 V1 T0 E2 O0 T1 V2 T2 O1 E3 H0 T3 V3 E4 O2 O3 E5 T4 K0 T5 E6 K1 X0 Y0 O4 T6 E7 O5 T7
        H1 H2 O6 Y1 H3 X1 O7 K2 G0 Y2 F0 X2 K3 X3 F1 Y3 F2 G1 G2 F3 G3"""
    DVE_ORDER = """M0 M1 L0 V0 M2 T0 V1 L1 T1 C0 M3 R0 V2 L2 T2 M4 C1 V3 T3 R1 N0 M5 C2 C3 R2 R3 N1 M6 T4 T5 M7
        X0 Y0 C4 R4 T6 C5 L3 R5 T7 C6 N2 R6 X1 Y1 C7 F0 R7 N3 G0 Y2 F1 U0 X2 Z0 X3 F2 U1 Y3 U2 Z1 G1
        F3 Z2 U3 G2 G3 Z3"""
    POOL_ORDER = """C0 L0 L1 C1 C2 C3 N0 N1 C4 L2 C5 L3 C6 N2 C7 N3 U0 U1 U2 U3"""

    PE_LAST = """V0 S0 V1 S1 T0 S2 V2 T1 S3 O0 T2 O1 S4 T3 S5 O2 T4 O3 S6 V3 T5 O4 S7 Y0 T6 O5 T7 O6 Y1 F0 O7
        Y2 F1 F2 Y3 D11 Y4 F3 D12 F4"""
    ACT_LAST = """E0 V0 V1 T0 E1 V2 T1 E2 O0 E3 T2 O1 T3 E4 T4 O2 O3 E5 K0 E6 V3 T5 O4 Y0 T6 E7 O5 K1 T7 O6 Y1
        K2 F0 O7 Y2 K3 Y3 F1 K4 Y4 F2 F3 F4"""
    DVE_LAST = """M0 V0 M1 M2 V1 T0 V2 T1 C0 M3 M4 C1 R0 T2 R1 T3 N0 M5 C2 R2 C3 T4 M6 R3 V3 N1 C4 T5 R4 M7 Y0
        T6 C5 R5 T7 N2 C6 F0 R6 Y1 U0 N3 C7 Y2 F1 R7 N4 F2 Y3 U1 Z0 Z1 Y4 U2 F3 U3 F4 Z2 U4 Z3 Z4"""
    POOL_LAST = """C0 C1 C2 N0 C3 N1 C4 C5 N2 C6 U0 N3 C7 N4 U1 U2 U3 U4"""

    PE_BEFORE = "D22 W0 W1 D13 X0 A0 X1 D25 W2 G0 D6 X2 X3 G1 A1 G2 G3"
    ACT_BEFORE = "W0 H0 J0 H1 X0 A0 X1 B0 H2 H3 G0 J1 X2 X3 G1 U0 A1 U1 G2 U2 G3 E0"
    DVE_BEFORE = "L0 L1 W1 B0 J0 L2 L3 X0 A0 X1 W2 B1 G0 X2 X3 U0 G1 A1 U1 G2 G3"

    def steps_of(text):
        return [(w[0], int(w[1:])) for w in text.split()]

    def tiles_of(unit, last):
        if not last or unit < NP - 1:
            return 2 * unit, 2 * unit + 2, unit
        t = NT - NP + unit - 1
        return t, t + 1, t // 2

    def t_groups(i):
        n = i + 1
        return [(0, n)] if n <= 4 else [(0, (n + 1) // 2), ((n + 1) // 2, n)]

    def pieces(i):
        w = (i + 1) * PART
        return (1, w) if w <= BANK else (2, w // 2)

    def jobs_of(steps):
        for kind, n in steps:
            if kind == "T":
                for g in range(len(t_groups(n))):
                    yield (kind, n, g)
            elif kind in "VOYFXGA":
                yield (kind, n, 0)

    SPLIT = "ATVYXG"
    def is_split(job):
        return job[0] in SPLIT

    def places(jobs, act_jobs, job0, split0):
        splits = {j: split0 + 1 + at for at, j in enumerate(filter(is_split, act_jobs))}
        return {j: (job0 + at, splits.get(j, 0)) for at, j in enumerate(jobs)}

    before = places(jobs_of(steps_of(PE_BEFORE)), jobs_of(steps_of(ACT_BEFORE)), 0, 0)
    JOB0, SPLIT0 = len(before), sum(map(is_split, before))
    full, final = (places(jobs_of(steps_of(pe)), jobs_of(steps_of(act)), JOB0, SPLIT0)
                   for pe, act in ((PE_ORDER, ACT_ORDER), (PE_LAST, ACT_LAST)))
    PER, SPER = len(full), sum(map(is_split, full))
    assert PER % NB == 0

    class Job:

        def __init__(self, b, last, kind, n, g=0, before=0):
            place, splits = (final if last else full)[(kind, n, g)]
            self.bank = place % NB
            self.offset = place // NB - before * (PER // NB)
            self.used = self.offset + b * (PER // NB)
            self.splits = splits + b * SPER

    class Before:
        def __init__(self, kind, n):
            place, self.splits = before[(kind, n, 0)]
            self.bank, self.offset = place % NB, place // NB
            self.used = self.offset

    def g_job(b, n):
        return Before("G", n) if isinstance(b, int) and b == 0 else Job(b, False, "G", n, before=1)

    x_rows = x.rearrange("b (t p) d -> b p t d", p=PART)
    out_rows = out.rearrange("b (t p) d -> b p t d", p=PART)

    ctx = ExitStack()
    with ctx:
        def sb(name, shape, dt=f32):
            return ctx.enter_context(nc.sbuf_tensor(name, shape, dt))

        def pb(name, shape, dt=f32):
            return ctx.enter_context(nc.psum_tensor(name, shape, dt))

        def sem(name):
            return ctx.enter_context(nc.semaphore(name))

        x_sb = sb("x_sb", [PART, 2 * PAR])
        xn = sb("xn", [PART, NT, D])
        xT_hi = sb("xT_hi", [PART, KC, S], f32r)
        xT_lo = sb("xT_lo", [PART, KC, S], f32r)
        xT_first = sb("xT_first", [PART, KC, PART])
        g_first = sb("g_first", [PART, KC, PART])
        g_hi = sb("g_hi", [PART, KC, S], f32r)
        g_lo = sb("g_lo", [PART, KC, S], f32r)
        v_hi = sb("v_hi", [PART, NT, D], f32r)
        v_lo = sb("v_lo", [PART, NT, D], f32r)
        neg_scores = sb("neg_scores", [PART, 2, S])
        probs = sb("probs", [PART, 2, S])
        pT_hi = sb("pT_hi", [PART, 2, S], f32r)
        pT_lo = sb("pT_lo", [PART, 2, S], f32r)
        y = sb("y", [PART, NT, D])
        yn = sb("yn", [PART, NP, 2, D])
        yT_hi = sb("yT_hi", [PART, NP, KC, 2, PART], f32r)
        yT_lo = sb("yT_lo", [PART, NP, KC, 2, PART], f32r)
        f_sb = sb("f_sb", [PART, NP, 2, D])
        out_sb = sb("out_sb", [PART, NP, 2, D])
        squares_junk = sb("squares_junk", [PART, 2, NT, D], bf16)
        neg_max = sb("neg_max", [PART, NT])
        exp_sums = sb("exp_sums", [PART, NT])
        x_stats = sb("x_stats", [PART, NT, 6])
        x_mv = sb("x_mv", [PART, NT, 2])
        x_ve = sb("x_ve", [PART, NT])
        x_nm = sb("x_nm", [PART, NT])
        x_rstd = sb("x_rstd", [PART, NT])
        x_shift = sb("x_shift", [PART, NT])
        o_ss = sb("o_ss", [PART, NT])
        o_ez = sb("o_ez", [PART, NT])
        o_ve = sb("o_ve", [PART, NT])
        o_rstd = sb("o_rstd", [PART, NT])
        y_stats = sb("y_stats", [PART, NT, 6])
        y_mv = sb("y_mv", [PART, NT, 2])
        y_ve = sb("y_ve", [PART, NT])
        y_nm = sb("y_nm", [PART, NT])
        y_shift = sb("y_shift", [PART, NT])
        y_rstd = sb("y_rstd", [PART, NT])
        f_ss = sb("f_ss", [PART, NT])
        f_ve = sb("f_ve", [PART, NT])
        f_rstd = sb("f_rstd", [PART, NT])
        minus_half = sb("minus_half", [PART, NT])
        wq = sb("wq", [PART, KC, D])
        wk = sb("wk", [PART, KC, D])
        wv = sb("wv", [PART, KC, D])
        wo = sb("wo", [PART, KC, D])
        wT = sb("wT", [PART, 3, KC, D])
        a_hi = sb("a_hi", [PART, KC, D], f32r)
        a_lo = sb("a_lo", [PART, KC, D], f32r)
        wo_raw = sb("wo_raw", [PART, KC, D])
        wvo_hi = sb("wvo_hi", [PART, KC, D], f32r)
        wvo_lo = sb("wvo_lo", [PART, KC, D], f32r)
        wf = sb("wf", [PART, KC, D])
        wf_hi = sb("wf_hi", [PART, KC, D], f32r)
        wf_lo = sb("wf_lo", [PART, KC, D], f32r)
        bias = sb("bias", [PART, D])
        wf_raw = sb("wf_raw", [PART, KC, D])
        bias_raw = sb("bias_raw", [PART, D])
        row_sum = sb("row_sum", [PART, 5])
        neg_mean = sb("neg_mean", [PART, 5])
        sums_junk = sb("sums_junk", [PART, 5, D], bf16)
        ident = sb("ident", [PART, PART])
        mask = sb("mask", [PART, S])
        warm_b = sb("warm_b", [PART, PART], bf16)
        exp_junk = sb("exp_junk", [PART, 1])
        logits = sb("logits", [1, NOPS])
        noise_u = sb("noise_u", [1, NOPS])
        log_u = sb("log_u", [1, NOPS])
        neg_gumbel = sb("neg_gumbel", [1, NOPS])
        exp_logits = sb("exp_logits", [1, NOPS])
        lse = sb("lse", [1, 3])
        noisy = sb("noisy", [1, NOPS])
        top8 = sb("top8", [1, 8])
        chosen = sb("chosen", [1, 8], u32)

        score = pb("score", [PART, 2, 2, BANK])
        bank = [pb(f"bank{i}", [PART, BANK]) for i in range(NB)]

        bank_full = [sem(f"bank_full{i}") for i in range(NB)]
        bank_drained = [sem(f"bank_drained{i}") for i in range(NB)]
        hi_ready = sem("hi_ready")
        scores_ready = sem("scores_ready")
        max_ready = sem("max_ready")
        probs_ready = sem("probs_ready")
        o_squares = sem("o_squares")
        o_ve_ready = sem("o_ve_ready")
        o_rstd_ready = sem("o_rstd_ready")
        y_mv_ready = sem("y_mv_ready")
        y_ve_ready = sem("y_ve_ready")
        y_shift_ready = sem("y_shift_ready")
        yn_ready = sem("yn_ready")
        f_squares = sem("f_squares")
        f_ve_ready = sem("f_ve_ready")
        f_rstd_ready = sem("f_rstd_ready")
        out_ready = sem("out_ready")
        out_sent = [sem(f"out_sent{i}") for i in range(NP)]
        x_loaded = [sem(f"x_loaded{i}") for i in range(NP)]
        x_mv_ready = sem("x_mv_ready")
        x_ve_ready = sem("x_ve_ready")
        x_shift_ready = sem("x_shift_ready")
        xn_ready = sem("xn_ready")
        wq_loaded = sem("wq_loaded")
        wk_loaded = sem("wk_loaded")
        wv_loaded = sem("wv_loaded")
        wo_loaded = sem("wo_loaded")
        choice_loaded = sem("choice_loaded")
        wf_loaded = sem("wf_loaded")
        halves_ready = sem("halves_ready")
        memsets = sem("memsets")
        consts_ready = sem("consts_ready")
        mask_ready = sem("mask_ready")
        w_transposed = sem("w_transposed")
        wT_ready = sem("wT_ready")
        wqT_ready = sem("wqT_ready")
        row_sums_ready = sem("row_sums_ready")
        neg_means_ready = sem("neg_means_ready")
        wo_ready = sem("wo_ready")
        wf_centred = sem("wf_centred")
        wf_hi_ready = sem("wf_hi_ready")
        wf_ready = sem("wf_ready")
        choice_steps = sem("choice_steps")
        choice_act = sem("choice_act")
        choice_dve = sem("choice_dve")
        chosen_ready = sem("chosen_ready")

        block = ctx.enter_context(nc.Block())

        def cols(bk, n=BANK):
            return bank[bk][:, 0:n]

        def x_tile(b, t, n=1):
            return x_sb[:, bass.ds((b % 2) * PAR + t * D, n * D)]

        @block.sync
        def _(sp):
            def load_x(b, p, parity_at):
                sp.dma_start(x_sb[:, bass.ds(parity_at + 2 * p * D, 2 * D)],
                             x_rows[b, :, 2 * p:2 * p + 2, :]).then_inc(x_loaded[p], 16)

            def store(b, unit, last=False):
                sp.wait_ge(out_ready, b * NP + unit + 1)
                t0, t1, p = tiles_of(unit, last)
                sp.dma_start(out_rows[b, :, t0:t1, :], out_sb[:, p, t0 % 2:t0 % 2 + t1 - t0]).then_inc(out_sent[p], 16)

            def weight(w_sb, w_dram, loaded):
                sp.dma_start(w_sb[:, :, :], w_dram.rearrange("(k p) n -> p k n", p=PART)).then_inc(loaded, 16)

            load_x(0, 0, 0)
            sp.dma_start(wk[:, :, :], Wk.rearrange("(k p) n -> p k n", p=PART)).then_inc(wk_loaded, 16)
            load_x(0, 1, 0)
            sp.dma_start(logits[:, :], ffn_logits[None, :]).then_inc(choice_loaded, 16)
            sp.dma_start(noise_u[:, :], ffn_u[None, :]).then_inc(choice_loaded, 16)
            sp.dma_start(wv[:, :, :], Wv.rearrange("(k p) n -> p k n", p=PART)).then_inc(wv_loaded, 16)
            sp.dma_start(wo_raw[:, :, :], Wo.rearrange("(k p) n -> p k n", p=PART)).then_inc(wo_loaded, 16)
            load_x(0, 2, 0)
            load_x(0, 3, 0)
            sp.wait_ge(chosen_ready, 1)
            op = sp.value_load(chosen[0:1, 0:1], min_val=0, max_val=NOPS - 1)
            sp.dma_start(wf_raw[:, :, :], ffn_W[bass.ds(op, 1), :, :].rearrange("o (k p) n -> p (o k) n", p=PART)
                         ).then_inc(wf_loaded, 16)
            sp.dma_start(bias_raw[:, :], ffn_b[bass.ds(op, 1), :].broadcast_to([PART, D])).then_inc(wf_loaded, 16)
            for p in range(NP):
                sp.wait_ge(x_loaded[p], 16)
                load_x(1, p, PAR)

            def load_after(b, p):
                added = Job(b, False, "O", 2 * p + 1)
                sp.wait_ge(bank_drained[added.bank], added.used + 1)
                load_x(b + 2, p, (b % 2) * PAR)

            def sequence(b):
                for p in range(NP):
                    load_after(b, p)
                for p in range(NP):
                    store(b, p)

            sequence(0)
            with sp.Fori(1, B - 2) as b:
                sequence(b)
            for p in range(NP):
                store(B - 2, p)
            for unit in range(NP + 1):
                store(B - 1, unit, last=True)
            for p in range(NP):
                sp.wait_ge(out_sent[p], 16 * (B + (p == NP - 1)))

        @block.gpsimd
        def _(pool):
            nc.gpsimd.memset(minus_half[:, :], -0.5).then_inc(halves_ready, 1)
            nc.gpsimd.memset(warm_b[:, :], 0.0)
            nc.gpsimd.memset(ident[:, :], 0.0).then_inc(memsets, 1)
            pool.wait_ge(memsets, 1)
            nc.gpsimd.affine_select(out=ident[:, :], in_=ident[:, :], compare_op=ALU.not_equal, fill=1.0, base=0,
                                    pattern=[[-1, PART]], channel_multiplier=1).then_inc(consts_ready, 1)
            nc.gpsimd.memset(mask[:, :], 0.0).then_inc(memsets, 1)
            pool.wait_ge(memsets, 2)
            nc.gpsimd.affine_select(out=mask[:, S - PART:S], in_=mask[:, S - PART:S], compare_op=ALU.is_ge, fill=MASKED,
                                    base=0, pattern=[[-1, PART]], channel_multiplier=1).then_inc(mask_ready, 1)

            def rstd(dst, ve, n0, n1):
                return nc.gpsimd.tensor_tensor(dst[:, n0:n1], ve[:, n0:n1], minus_half[:, n0:n1], ALU.pow)

            def scales(nm, ve, rstds, shift, t0, t1):
                rstd(rstds, ve, t0, t1)
                pool.drain()
                return nc.gpsimd.tensor_tensor(shift[:, t0:t1], nm[:, t0:t1], rstds[:, t0:t1], ALU.mult)

            def x_scales(b, p):
                pool.wait_ge(x_ve_ready, b * NP + p + 1)
                scales(x_nm, x_ve, x_rstd, x_shift, 2 * p, 2 * p + 2).then_inc(x_shift_ready, 1)

            def sequence(b, last_one=False):
                for kind, n in steps_of(POOL_LAST if last_one else POOL_ORDER):
                    if kind in "NU":
                        t0, t1, _pair = tiles_of(n, last_one)
                    if kind == "L":
                        x_scales(b + 1, n)
                    elif kind == "C":
                        pool.wait_ge(o_ve_ready, b * NT + n + 1)
                        rstd(o_rstd, o_ve, n, n + 1).then_inc(o_rstd_ready, 1)
                    elif kind == "N":
                        pool.wait_ge(y_ve_ready, b * NP + n + 1)
                        scales(y_nm, y_ve, y_rstd, y_shift, t0, t1).then_inc(y_shift_ready, 1)
                    elif kind == "U":
                        pool.wait_ge(f_ve_ready, b * NP + n + 1)
                        rstd(f_rstd, f_ve, t0, t1).then_inc(f_rstd_ready, 1)

            for p in range(NP):
                x_scales(0, p)
            sequence(0)
            with pool.Fori(1, B - 1) as b:
                sequence(b)
            sequence(B - 1, True)

        @block.scalar
        def _(act):
            act.dma_start(wq[:, :, :], Wq.rearrange("(k p) n -> p k n", p=PART)).then_inc(wq_loaded, 16)

            def load_exp_table():
                nc.scalar.activation(exp_junk[:, :], minus_half[:, 0:1], ACT.Exp)

            act.wait_ge(halves_ready, 1)
            load_exp_table()

            def round_hi(job, dst, src):
                act.wait_ge(bank_full[job.bank], job.used + 1)
                nc.scalar.activation(dst, src, ACT.Identity).then_inc(hi_ready, 1)

            def keep_first(job, dst, src):
                act.wait_ge(bank_full[job.bank], job.used + 1)
                nc.scalar.activation(dst, src, ACT.Identity)

            def x_hi(job, p):
                if p == 0:
                    keep_first(job, xT_first[:, :, :], cols(job.bank).rearrange("p (k s) -> p k s", k=KC)[:, :, 0:PART])
                round_hi(job, xT_hi[:, :, 2 * p * PART:2 * (p + 1) * PART],
                         cols(job.bank).rearrange("p (k s) -> p k s", k=KC))

            def g_hi_quarter(job, n):
                c, m = n // 2, n % 2
                if c == 0:
                    keep_first(job, g_first[:, m, :], cols(job.bank, PART))
                round_hi(job, g_hi[:, m, c * BANK:(c + 1) * BANK], cols(job.bank))

            def normalise_x(b, p):
                act.wait_ge(x_shift_ready, b * NP + p + 1)
                for t in (2 * p, 2 * p + 1):
                    last = nc.scalar.activation(xn[:, t, :], x_tile(b, t), ACT.Identity, bias=x_shift[:, t:t + 1],
                                                scale=x_rstd[:, t:t + 1])
                last.then_inc(xn_ready, 1)

            def row_sums(n, w):
                return nc.scalar.activation(sums_junk[:, n, :], w, ACT.Identity, accum_out=row_sum[:, n:n + 1])

            def centred(n, w_raw, w):
                return nc.scalar.activation(w, w_raw, ACT.Identity, bias=neg_mean[:, n:n + 1])

            def choice():
                act.wait_ge(choice_loaded, 32)
                act.wait_ge(choice_dve, 1)
                nc.scalar.activation(exp_logits[:, :], logits[:, :], ACT.Exp, bias=lse[:, 0:1], accum_out=lse[:, 1:2])
                nc.scalar.activation(log_u[:, :], noise_u[:, :], ACT.Ln).then_inc(choice_act, 1)
                act.wait_ge(choice_act, 1)
                nc.scalar.activation(lse[:, 2:3], lse[:, 1:2], ACT.Ln)
                nc.scalar.activation(neg_gumbel[:, :], log_u[:, :], ACT.Ln, scale=-1.0).then_inc(choice_act, 1)

            def ffn_weights(step):
                if step == 0:
                    act.wait_ge(wf_loaded, 32)
                    for m in range(KC):
                        row_sums(2 + m, wf_raw[:, m, :])
                    row_sums(4, bias_raw[:, :]).then_inc(row_sums_ready, 1)
                elif step == 1:
                    act.wait_ge(neg_means_ready, 2)
                    for m in range(KC):
                        centred(2 + m, wf_raw[:, m, :], wf[:, m, :])
                    centred(4, bias_raw[:, :], bias[:, :]).then_inc(wf_centred, 1)
                else:
                    act.wait_ge(wf_centred, 1)
                    nc.scalar.activation(wf_hi[:, :, :], wf[:, :, :], ACT.Identity).then_inc(wf_hi_ready, 1)

            for kind, n in steps_of(ACT_BEFORE):
                if kind == "W":
                    act.wait_ge(w_transposed, 1)
                    nc.scalar.activation(wT[:, 0, :, :].rearrange("p k n -> p (k n)"), score[:, 0, 0, :],
                                         ACT.Identity).then_inc(wqT_ready, 1)
                elif kind == "H":
                    normalise_x(0, n)
                elif kind == "J" and n == 0:
                    act.wait_ge(wo_loaded, 16)
                    row_sums(0, wo_raw[:, 0, :])
                    row_sums(1, wo_raw[:, 1, :]).then_inc(row_sums_ready, 1)
                elif kind == "J":
                    act.wait_ge(neg_means_ready, 1)
                    centred(0, wo_raw[:, 0, :], wo[:, 0, :])
                    centred(1, wo_raw[:, 1, :], wo[:, 1, :]).then_inc(wo_ready, 1)
                elif kind == "B":
                    choice()
                elif kind == "E":
                    load_exp_table()
                elif kind == "U":
                    ffn_weights(n)
                elif kind == "X":
                    x_hi(Before("X", n), n)
                elif kind == "G":
                    g_hi_quarter(Before("G", n), n)
                elif kind == "A":
                    job = Before("A", n)
                    act.wait_ge(bank_full[job.bank], job.used + 1)
                    nc.scalar.activation((wvo_hi if n else a_hi)[:, :, :],
                                         cols(job.bank).rearrange("p (m n) -> p m n", m=KC), ACT.Identity, scale=1.0 if n else -SCALE).then_inc(hi_ready, 1)

            def sequence(b, last_one=False):
                def at(kind, n, g=0):
                    return Job(b, last_one, kind, n, g)

                for kind, n in steps_of(ACT_LAST if last_one else ACT_ORDER):
                    if kind in "NKYFUZ":
                        t0, t1, p = tiles_of(n, last_one)
                        here = slice(t0 % 2, t0 % 2 + t1 - t0)
                    if kind == "E":
                        act.wait_ge(max_ready, b * NT + n + 1)
                        here = slice(0, (n + 1) * PART)
                        nc.scalar.activation(probs[:, n % 2, here], neg_scores[:, n % 2, here], ACT.Exp, scale=-1.0,
                                             bias=neg_max[:, n:n + 1],
                                             accum_out=exp_sums[:, n:n + 1]).then_inc(probs_ready, 1)
                    elif kind == "T":
                        for g, (t0, t1) in enumerate(t_groups(n)):
                            job = at("T", n, g)
                            round_hi(job, pT_hi[:, n % 2, t0 * PART:t1 * PART], cols(job.bank, (t1 - t0) * PART))
                    elif kind == "V":
                        job = at("V", n)
                        round_hi(job, v_hi[:, 2 * n:2 * n + 2, 0:D],
                                 cols(job.bank).rearrange("p (t d) -> p t d", t=2))
                    elif kind == "Y":
                        job = at("Y", n)
                        round_hi(job, yT_hi[:, p, :, here, :], cols(job.bank, KC * (t1 - t0) * PART).rearrange(
                            "p (k t s) -> p k t s", k=KC, t=t1 - t0))
                    elif kind == "H":
                        normalise_x(b + 1, n)
                    elif kind == "X":
                        x_hi(at("X", n), n)
                    elif kind == "G":
                        g_hi_quarter(at("G", n), n)
                    elif kind == "O":
                        job = at("O", n)
                        act.wait_ge(bank_full[job.bank], job.used + 1)
                        nc.scalar.activation(squares_junk[:, 0, n, :], cols(job.bank, D), ACT.Square,
                                             accum_out=o_ss[:, n:n + 1])
                        nc.scalar.activation(o_ez[:, n:n + 1], exp_sums[:, n:n + 1], ACT.Square,
                                             scale=EPS ** 0.5).then_inc(o_squares, 1)
                    elif kind == "K":
                        act.wait_ge(y_shift_ready, b * NP + n + 1)
                        for t in range(t0, t1):
                            last = nc.scalar.activation(yn[:, p, t % 2, :], y[:, t, :], ACT.Identity,
                                                        bias=y_shift[:, t:t + 1], scale=y_rstd[:, t:t + 1])
                        last.then_inc(yn_ready, 1)
                    elif kind == "F":
                        job = at("F", n)
                        act.wait_ge(bank_drained[job.bank], job.used + 1)
                        for t in range(t0, t1):
                            last = nc.scalar.activation(squares_junk[:, 1, t, :], f_sb[:, p, t % 2, :], ACT.Square,
                                                        accum_out=f_ss[:, t:t + 1])
                        last.then_inc(f_squares, 1)

            sequence(0)
            with act.Fori(1, B - 1) as b:
                sequence(b)
            sequence(B - 1, True)

        @block.vector
        def _(dve):
            links = [0]

            def link(ins):
                links[0] += 1
                ins.then_inc(choice_steps, 1)
                dve.wait_ge(choice_steps, links[0])

            def subtract_lo(job, dst, hi, src):
                dve.wait_ge(hi_ready, job.splits)
                nc.vector.tensor_tensor(dst, src, hi.bitcast(f32), ALU.subtract).then_inc(bank_drained[job.bank], 1)

            def x_lo(job, p):
                here = slice(2 * p * PART, 2 * (p + 1) * PART)
                subtract_lo(job, xT_lo[:, :, here], xT_hi[:, :, here], cols(job.bank).rearrange("p (k s) -> p k s", k=KC))

            def g_lo_quarter(job, n):
                m, here = n % 2, slice(n // 2 * BANK, (n // 2 + 1) * BANK)
                subtract_lo(job, g_lo[:, m, here], g_hi[:, m, here], cols(job.bank))

            def x_statistics(b, p):
                dve.wait_ge(x_loaded[p], 16 * (b + 1))
                for t in (2 * p, 2 * p + 1):
                    nc.vector.bn_stats(x_stats[:, t, :], x_tile(b, t))
                dve.drain()
                for t in (2 * p, 2 * p + 1):
                    last = nc.vector.bn_aggr(x_mv[:, t, :], x_stats[:, t, :])
                last.then_inc(x_mv_ready, 1)
                dve.wait_ge(x_mv_ready, b * NP + p + 1)
                nc.vector.tensor_scalar(x_nm[:, 2 * p:2 * p + 2], x_mv[:, 2 * p:2 * p + 2, 0], -1.0, None, ALU.mult)
                nc.vector.tensor_scalar(x_ve[:, 2 * p:2 * p + 2], x_mv[:, 2 * p:2 * p + 2, 1], EPS, None,
                                        ALU.add).then_inc(x_ve_ready, 1)

            def copy_transposed(n):
                dve.wait_ge(w_transposed, n + 1)
                nc.vector.tensor_copy(wT[:, n, :, :].rearrange("p k n -> p (k n)"),
                                      score[:, n // 2, n % 2, :]).then_inc(wT_ready, 1)

            def negative_means(n0, n1, k):
                dve.wait_ge(row_sums_ready, k)
                nc.vector.tensor_scalar(neg_mean[:, n0:n1], row_sum[:, n0:n1], -1.0 / D, None,
                                        ALU.mult).then_inc(neg_means_ready, 1)

            for kind, n in steps_of(DVE_BEFORE):
                if kind == "L":
                    x_statistics(0, n)
                elif kind == "W":
                    copy_transposed(n)
                elif kind == "J":
                    negative_means(0, 2, 1)
                elif kind == "U" and n == 0:
                    negative_means(2, 5, 2)
                elif kind == "U":
                    dve.wait_ge(wf_hi_ready, 1)
                    nc.vector.tensor_tensor(wf_lo[:, :, :], wf[:, :, :], wf_hi[:, :, :].bitcast(f32),
                                            ALU.subtract).then_inc(wf_ready, 1)
                elif kind == "B" and n == 0:
                    dve.wait_ge(choice_loaded, 32)
                    nc.vector.tensor_reduce(lse[:, 0:1], logits[:, :], AX.X, ALU.max, negate=True).then_inc(choice_dve, 1)
                elif kind == "B":
                    dve.wait_ge(choice_act, 2)
                    link(nc.vector.tensor_scalar(noisy[:, :], logits[:, :], lse[:, 0:1], lse[:, 2:3],
                                                 ALU.add, ALU.subtract))
                    link(nc.vector.tensor_tensor(noisy[:, :], noisy[:, :], neg_gumbel[:, :], ALU.subtract))
                    link(nc.vector.max(top8[:, :], noisy[:, :]))
                    nc.vector.max_index(chosen[:, :], top8[:, :], noisy[:, :]).then_inc(chosen_ready, 1)
                elif kind == "X":
                    x_lo(Before("X", n), n)
                elif kind == "G":
                    g_lo_quarter(Before("G", n), n)
                elif kind == "A":
                    job = Before("A", n)
                    dve.wait_ge(hi_ready, job.splits)
                    nc.vector.scalar_tensor_tensor(out=(wvo_lo if n else a_lo)[:, :, :],
                                                   in0=cols(job.bank).rearrange("p (m n) -> p m n", m=KC),
                                                   scalar=1.0 if n else -SCALE,
                                                   in1=(wvo_hi if n else a_hi)[:, :, :].bitcast(f32),
                                                   op0=ALU.mult, op1=ALU.subtract).then_inc(bank_drained[job.bank], 1)

            dve.wait_ge(mask_ready, 1)

            def sequence(b, last_one=False):
                def at(kind, n, g=0):
                    return Job(b, last_one, kind, n, g)

                for kind, n in steps_of(DVE_LAST if last_one else DVE_ORDER):
                    if kind in "NKYFUZ":
                        t0, t1, p = tiles_of(n, last_one)
                        here = slice(t0 % 2, t0 % 2 + t1 - t0)
                    if kind == "M":
                        dve.wait_ge(scores_ready, b * NT + n + 1)
                        h, w = pieces(n)
                        here = slice(S - h * w, S)
                        dve.nop(nofuse=True)
                        masked = neg_scores[:, n % 2, 0:h * w]
                        nc.vector.tensor_tensor_reduce(out=masked.rearrange("p (h w) -> p h w", h=h),
                                                       in0=score[:, n % 2, 0:h, 0:w],
                                                       in1=mask[:, here].rearrange("p (h w) -> p h w", h=h),
                                                       scale=1.0, scalar=3e38, op0=ALU.add, op1=ALU.min,
                                                       accum_out=neg_max[:, n:n + 1]).then_inc(max_ready, 1)
                    elif kind == "T":
                        for g, (t0, t1) in enumerate(t_groups(n)):
                            job, here = at("T", n, g), slice(t0 * PART, t1 * PART)
                            subtract_lo(job, pT_lo[:, n % 2, here], pT_hi[:, n % 2, here],
                                        cols(job.bank, (t1 - t0) * PART))
                    elif kind == "V":
                        job = at("V", n)
                        subtract_lo(job, v_lo[:, 2 * n:2 * n + 2, 0:D], v_hi[:, 2 * n:2 * n + 2, 0:D],
                                    cols(job.bank).rearrange("p (t d) -> p t d", t=2))
                    elif kind == "Y":
                        job = at("Y", n)
                        subtract_lo(job, yT_lo[:, p, :, here, :], yT_hi[:, p, :, here, :],
                                    cols(job.bank, KC * (t1 - t0) * PART).rearrange("p (k t s) -> p k t s", k=KC,
                                                                                    t=t1 - t0))
                    elif kind == "X":
                        x_lo(at("X", n), n)
                    elif kind == "G":
                        g_lo_quarter(at("G", n), n)
                    elif kind == "L":
                        x_statistics(b + 1, n)
                    elif kind == "C":
                        dve.wait_ge(o_squares, b * NT + n + 1)
                        nc.vector.tensor_scalar(o_ve[:, n:n + 1], o_ss[:, n:n + 1], 1.0 / D, o_ez[:, n:n + 1],
                                                ALU.mult, ALU.add).then_inc(o_ve_ready, 1)
                    elif kind == "R":
                        job = at("O", n)
                        dve.wait_ge(o_rstd_ready, b * NT + n + 1)
                        nc.vector.scalar_tensor_tensor(out=y[:, n, :], in0=cols(job.bank, D), scalar=o_rstd[:, n:n + 1],
                                                       in1=x_tile(b, n), op0=ALU.mult,
                                                       op1=ALU.add).then_inc(bank_drained[job.bank], 1)
                    elif kind == "N":
                        for t in range(t0, t1):
                            job = at("O", t)
                            dve.wait_ge(bank_drained[job.bank], job.used + 1)
                            nc.vector.bn_stats(y_stats[:, t, :], y[:, t, :])
                        dve.drain()
                        for t in range(t0, t1):
                            last = nc.vector.bn_aggr(y_mv[:, t, :], y_stats[:, t, :])
                        last.then_inc(y_mv_ready, 1)
                        dve.wait_ge(y_mv_ready, b * NP + n + 1)
                        nc.vector.tensor_scalar(y_nm[:, t0:t1], y_mv[:, t0:t1, 0], -1.0, None, ALU.mult)
                        nc.vector.tensor_scalar(y_ve[:, t0:t1], y_mv[:, t0:t1, 1], EPS, None,
                                                ALU.add).then_inc(y_ve_ready, 1)
                    elif kind == "F":
                        job = at("F", n)
                        dve.wait_ge(bank_full[job.bank], job.used + 1)
                        nc.vector.tensor_tensor(f_sb[:, p, here, :],
                                                cols(job.bank, (t1 - t0) * D).rearrange("p (t d) -> p t d", t=t1 - t0),
                                                bias[:, None, :].broadcast_to([PART, t1 - t0, D]),
                                                ALU.add).then_inc(bank_drained[job.bank], 1)
                    elif kind == "U":
                        dve.wait_ge(f_squares, b * NP + n + 1)
                        nc.vector.tensor_scalar(f_ve[:, t0:t1], f_ss[:, t0:t1], 1.0 / D, EPS, ALU.mult,
                                                ALU.add).then_inc(f_ve_ready, 1)
                    elif kind == "Z":
                        if not (isinstance(b, int) and b == 0):
                            dve.wait_ge(out_sent[p], b * 16)
                        dve.wait_ge(f_rstd_ready, b * NP + n + 1)
                        for t in range(t0, t1):
                            last = nc.vector.scalar_tensor_tensor(out=out_sb[:, p, t % 2, :], in0=f_sb[:, p, t % 2, :],
                                                                  scalar=f_rstd[:, t:t + 1], in1=y[:, t, :],
                                                                  op0=ALU.mult, op1=ALU.add)
                        last.then_inc(out_ready, 1)

            sequence(0)
            with dve.Fori(1, B - 1) as b:
                sequence(b)
            sequence(B - 1, True)

        @block.tensor
        def _(pe):
            def take_bank(job, *inputs):
                needed = {job.bank: (job.offset, job.used)} if job.offset else {}
                for done in inputs:
                    if done.offset + 1 > needed.get(done.bank, (0,))[0]:
                        needed[done.bank] = (done.offset + 1, done.used + 1)
                for bk, (_offset, used) in needed.items():
                    pe.wait_ge(bank_drained[bk], used)

            def product(dst, halves_l, halves_r):
                passes = [(l, r) for (l_hi, l_lo), (r_hi, r_lo) in zip(halves_l, halves_r)
                          for l, r in ((l_lo, r_hi), (l_hi, r_lo), (l_hi, r_hi))]
                for i, (l, r) in enumerate(passes):
                    last = nc.tensor.matmul(dst, l, r, start=(i == 0), stop=(i == len(passes) - 1))
                return last

            def both(hi, lo, *index):
                return hi[index], lo[index]

            ALL = slice(None)

            def x_transposes(b, job, p):
                pe.wait_ge(xn_ready, b * NP + p + 1)
                take_bank(job)
                for k in range(KC):
                    for t in range(2):
                        last = nc.tensor.transpose(cols(job.bank)[:, (2 * k + t) * PART:(2 * k + t + 1) * PART],
                                                   xn[:, 2 * p + t, k * PART:(k + 1) * PART], ident[:, :])
                last.then_inc(bank_full[job.bank], 1)

            def g_quarter(job, inputs, n):
                c, m = n // 2, n % 2
                take_bank(job, *inputs)
                product(cols(job.bank),
                        [both(a_hi, a_lo, ALL, k, slice(m * PART, (m + 1) * PART)) for k in range(KC)],
                        [both(xT_hi, xT_lo, ALL, k, slice(c * BANK, (c + 1) * BANK)) for k in range(KC)]
                        ).then_inc(bank_full[job.bank], 1)

            def keep_warm(passes):
                for _ in range(passes):
                    nc.tensor.matmul(score[:, 1, 1, 0:PART], warm_b[:, :], warm_b[:, :], start=True, stop=True)

            pe.wait_ge(consts_ready, 1)
            for kind, n in steps_of(PE_BEFORE):
                if kind == "D":
                    keep_warm(n)
                elif kind == "W":
                    w, loaded = ((wq, wq_loaded), (wk, wk_loaded), (wv, wv_loaded))[n]
                    pe.wait_ge(loaded, 16)
                    for k in range(KC):
                        for m in range(KC):
                            last = nc.tensor.transpose(score[:, n // 2, n % 2, (2 * k + m) * PART:(2 * k + m + 1) * PART],
                                                       w[:, m, k * PART:(k + 1) * PART], ident[:, :])
                    last.then_inc(w_transposed, 1)
                elif kind == "X":
                    x_transposes(0, Before("X", n), n)
                elif kind == "G":
                    g_quarter(Before("G", n), [Before("A", 0), Before("X", 2 * (n // 2)), Before("X", 2 * (n // 2) + 1)], n)
                elif kind == "A":
                    pe.wait_ge(wqT_ready, 1)
                    pe.wait_ge(wT_ready, 1 + n)
                    if n:
                        pe.wait_ge(wo_ready, 1)
                    job = Before("A", n)
                    take_bank(job)
                    for m in range(KC):
                        for k in range(KC):
                            last = nc.tensor.matmul(cols(job.bank)[:, m * D:(m + 1) * D],
                                                    wT[:, 2 * n, k, m * PART:(m + 1) * PART],
                                                    wo[:, k, :] if n else wT[:, 1, k, :],
                                                    start=(k == 0), stop=(k == KC - 1))
                    last.then_inc(bank_full[job.bank], 1)
            wvo_job = Before("A", 1)
            pe.wait_ge(bank_drained[wvo_job.bank], wvo_job.used + 1)

            def sequence(b, last_one=False, first=False):
                def at(kind, n, g=0):
                    return Job(b, last_one, kind, n, g)

                for kind, n in steps_of(PE_LAST if last_one else PE_ORDER):
                    if kind in "NKYFUZ":
                        t0, t1, p = tiles_of(n, last_one)
                        here = slice(t0 % 2, t0 % 2 + t1 - t0)
                    if kind == "S":
                        if n == 0 or n == NT // 2:
                            g = g_job(b, 2 * (n // (NT // 2)) + 1)
                            pe.wait_ge(bank_drained[g.bank], g.used + 1)
                        h, w = pieces(n)
                        if w < 2 * PART:
                            for k in range(KC):
                                last = nc.tensor.matmul(score[:, 0, 0, 0:PART], g_first[:, k, :], xT_first[:, k, :],
                                                        start=(k == 0), stop=(k == KC - 1))
                        else:
                            for piece in range(h):
                                last = product(score[:, n % 2, piece, 0:w],
                                               [both(g_hi, g_lo, ALL, k, slice(n * PART, (n + 1) * PART))
                                                for k in range(KC)],
                                               [both(xT_hi, xT_lo, ALL, k, slice(piece * w, (piece + 1) * w))
                                                for k in range(KC)])
                        last.then_inc(scores_ready, 1)
                    elif kind == "T":
                        pe.wait_ge(probs_ready, b * NT + n + 1)
                        for g, (t0, t1) in enumerate(t_groups(n)):
                            job = at("T", n, g)
                            take_bank(job)
                            for t in range(t0, t1):
                                last = nc.tensor.transpose(cols(job.bank)[:, (t - t0) * PART:(t - t0 + 1) * PART],
                                                           probs[:, n % 2, t * PART:(t + 1) * PART], ident[:, :])
                            last.then_inc(bank_full[job.bank], 1)
                    elif kind == "V":
                        job = at("V", n)
                        take_bank(job)
                        for t in (2 * n, 2 * n + 1):
                            last = product(cols(job.bank)[:, t % 2 * D:(t % 2 + 1) * D],
                                           [both(xT_hi, xT_lo, ALL, k, slice(t * PART, (t + 1) * PART)) for k in range(KC)],
                                           [both(wvo_hi, wvo_lo, ALL, k, ALL) for k in range(KC)])
                        last.then_inc(bank_full[job.bank], 1)
                    elif kind == "O":
                        job = at("O", n)
                        take_bank(job, at("T", n, len(t_groups(n)) - 1), at("V", n // 2))
                        product(cols(job.bank, D),
                                [both(pT_hi, pT_lo, ALL, n % 2, slice(t * PART, (t + 1) * PART)) for t in range(n + 1)],
                                [both(v_hi, v_lo, ALL, t, ALL) for t in range(n + 1)]
                                ).then_inc(bank_full[job.bank], 1)
                    elif kind == "Y":
                        pe.wait_ge(yn_ready, b * NP + n + 1)
                        job = at("Y", n)
                        take_bank(job)
                        for i, (k, t) in enumerate((k, t) for k in range(KC) for t in range(t0, t1)):
                            last = nc.tensor.transpose(cols(job.bank)[:, i * PART:(i + 1) * PART],
                                                       yn[:, p, t % 2, k * PART:(k + 1) * PART], ident[:, :])
                        last.then_inc(bank_full[job.bank], 1)
                    elif kind == "F":
                        if first and n == 0:
                            pe.wait_ge(wf_ready, 1)
                        job = at("F", n)
                        take_bank(job, at("Y", n))
                        for t in range(t0, t1):
                            last = product(cols(job.bank)[:, (t - t0) * D:(t - t0 + 1) * D],
                                           [both(yT_hi, yT_lo, ALL, p, k, t % 2, ALL) for k in range(KC)],
                                           [both(wf_hi, wf_lo, ALL, k, ALL) for k in range(KC)])
                        last.then_inc(bank_full[job.bank], 1)
                    elif kind == "D":
                        keep_warm(n)
                    elif kind == "X":
                        x_transposes(b + 1, at("X", n), n)
                    elif kind == "G":
                        g_quarter(at("G", n), [at("X", 2 * (n // 2) + 1)], n)

            sequence(0, first=True)
            with pe.Fori(1, B - 1) as b:
                sequence(b)
            sequence(B - 1, last_one=True)


_INS = ["L0_attn_x", "L0_attn_Wq", "L0_attn_Wk", "L0_attn_Wv", "L0_attn_Wo",
        "L0_ffn_W", "L0_ffn_b", "L0_ffn_logits", "L0_ffn_u"]
_OUTS = [((8, 1024, 256), "float32")]


def kernel(**inputs):
    import numpy as _np
    import concourse.bacc as _bacc
    from concourse import mybir as _mybir
    from concourse.bass_utils import run_bass_kernel_spmd as _run

    nc = _bacc.Bacc("TRN2", target_bir_lowering=False, num_devices=1)
    arrays, args = {}, []
    for name in _INS:
        a = _np.ascontiguousarray(inputs[name])
        arrays[f"in_{name}_dram"] = a
        args.append(nc.dram_tensor(f"in_{name}_dram", a.shape, _mybir.dt.from_np(a.dtype), kind="ExternalInput").ap())
    for i, (shape, dtype) in enumerate(_OUTS):
        dt = _mybir.dt.from_np(_np.dtype(dtype))
        args.append(nc.dram_tensor(f"out_{i}_dram", shape, dt, kind="ExternalOutput").ap())
    sandwich_block_kernel(nc, *args)
    r = _run(nc, [arrays], core_ids=[0])
    got = tuple(r.results[0][f"out_{i}_dram"] for i in range(len(_OUTS)))
    return got[0]
```
